# Optimizing a Trainium2 kernel written in Bass

```python
import numpy as np
import jax
import jax.numpy as jnp

def _softmax(x, axis=-1):
    return jax.nn.softmax(x, axis=axis)

def _gelu(x):
    return jax.nn.gelu(x, approximate=True)

def _silu(x):
    return jax.nn.silu(x)

def _sigmoid(x):
    return jax.nn.sigmoid(x)

def _layernorm(x, axis=-1, eps=1e-05):
    m = jnp.mean(x, axis=axis, keepdims=True)
    v = jnp.var(x, axis=axis, keepdims=True)
    return (x - m) / jnp.sqrt(v + eps)

def _scatter_add(tgt, idx, src, axis=0):
    return tgt.at[idx].add(src)

def _segment_sum(src, seg, n):
    return jax.ops.segment_sum(src, seg, n)
kernel_name = 'mk_cond_resid_d1_seqx_r4_6d75ab'

def setup_inputs(seed: int=0):
    np.random.seed(seed)
    _w = jnp.asarray

    def _rec_inputs():
        import jax
        import jax.numpy as jnp
        _rk = jax.random.key(seed)
        x = -0.000125 + 0.9999 * jax.random.normal(jax.random.fold_in(_rk, 1), (4, 512, 256), jnp.float32)
        _lenS = 512 - jax.random.randint(jax.random.fold_in(_rk, 7), (4,), 0, max(1, 512 // 4) + 1, jnp.int32)
        _lenS2 = 512 - jax.random.randint(jax.random.fold_in(_rk, 8), (4,), 0, max(1, 512 // 4) + 1, jnp.int32)
        cond_1024 = -0.00493535 + 1.00056 * jax.random.normal(jax.random.fold_in(_rk, 11), (4, 256), jnp.float32)
        return (x, cond_1024)
    x, cond_1024 = _rec_inputs()

    def _L0_cond_setup():
        import jax, jax.numpy as jnp
        import numpy as np
        D = 256
        H = 256
        N = 64
        T = 128

        def _lstm(x, h0, Wx, Wh, b):
            xW = jnp.einsum('ntd,dk->tnk', x, Wx) + b
            c0 = jnp.zeros_like(h0)
            Hdim = h0.shape[1]

            def step(carry, xw_t):
                prev_h, prev_c = carry
                a = xw_t + prev_h @ Wh
                i = jax.nn.sigmoid(a[:, 0:Hdim])
                f = jax.nn.sigmoid(a[:, Hdim:2 * Hdim])
                o = jax.nn.sigmoid(a[:, 2 * Hdim:3 * Hdim])
                g = jnp.tanh(a[:, 3 * Hdim:4 * Hdim])
                next_c = f * prev_c + i * g
                next_h = o * jnp.tanh(next_c)
                return ((next_h, next_c), next_h)
            _, hs = jax.lax.scan(step, (h0, c0), xW)
            return jnp.transpose(hs, (1, 0, 2))
        key = jax.random.key(seed)
        k1, k2, k3, k4 = jax.random.split(key, 4)
        x = jax.random.normal(k1, (N, T, D), dtype=jnp.float32)
        h0 = jax.random.normal(k2, (N, H), dtype=jnp.float32)
        Wx = jax.random.normal(k3, (D, 4 * H), dtype=jnp.float32) / np.sqrt(D)
        Wh = jax.random.normal(k4, (H, 4 * H), dtype=jnp.float32) / np.sqrt(H)
        b = jnp.zeros((4 * H,), dtype=jnp.float32)
        return {'x': x, 'h0': h0, 'Wx': Wx, 'Wh': Wh, 'b': b}
    _L0_cond_all = _L0_cond_setup()
    _L0_cond_in = {k: v for k, v in _L0_cond_all.items() if k in ('Wx', 'Wh', 'b')}
    del _L0_cond_all
    return {'x': x, 'cond_1024': cond_1024, 'L0_cond_Wx': _L0_cond_in['Wx'], 'L0_cond_Wh': _L0_cond_in['Wh'], 'L0_cond_b': _L0_cond_in['b']}

def reference(x, cond_1024, L0_cond_Wx, L0_cond_Wh, L0_cond_b):
    import jax
    import jax.numpy as jnp

    def _L0_cond_ref(x, h0, Wx, Wh, b):
        import jax, jax.numpy as jnp
        import numpy as np
        D = 256
        H = 256
        N = 64
        T = 128

        def _lstm(x, h0, Wx, Wh, b):
            xW = jnp.einsum('ntd,dk->tnk', x, Wx) + b
            c0 = jnp.zeros_like(h0)
            Hdim = h0.shape[1]

            def step(carry, xw_t):
                prev_h, prev_c = carry
                a = xw_t + prev_h @ Wh
                i = jax.nn.sigmoid(a[:, 0:Hdim])
                f = jax.nn.sigmoid(a[:, Hdim:2 * Hdim])
                o = jax.nn.sigmoid(a[:, 2 * Hdim:3 * Hdim])
                g = jnp.tanh(a[:, 3 * Hdim:4 * Hdim])
                next_c = f * prev_c + i * g
                next_h = o * jnp.tanh(next_c)
                return ((next_h, next_c), next_h)
            _, hs = jax.lax.scan(step, (h0, c0), xW)
            return jnp.transpose(hs, (1, 0, 2))
        return _lstm(x, h0, Wx, Wh, b)
    x = x + _L0_cond_ref(x, cond_1024, L0_cond_Wx, L0_cond_Wh, L0_cond_b)
    return x

_drawn_inputs = setup_inputs


def setup_inputs(seed=0):
    import zlib

    import numpy as np

    out = dict(_drawn_inputs(seed))
    spreads = {'L0_cond_b': (0.0, 0.1)}
    factors = {}
    for name, (base, spread) in spreads.items():
        noise = np.random.default_rng([zlib.crc32(name.encode()), seed]).standard_normal(out[name].shape)
        drawn = base * np.exp(spread * noise) if base else spread * noise
        out[name] = jnp.asarray(drawn.astype(out[name].dtype))
    for name, factor in factors.items():
        out[name] = (out[name] * factor).astype(out[name].dtype)
    return out
```

```python
import concourse.bass as bass
from concourse import mybir
from contextlib import ExitStack


def lstm_residual_kernel(nc: bass.Bass, x: bass.AP, cond: bass.AP, w_x: bass.AP, w_h: bass.AP, bias: bass.AP,
                         out: bass.AP):
    f32 = mybir.dt.float32
    ACT = mybir.ActivationFunctionType
    ALU = mybir.AluOpType

    N, T, D = x.shape
    Q, M, R = 4, 2, 32
    QD = M * R
    STEPS = R // N
    GATES = ("o", "i", "f", "g")
    SOURCE = {"i": 0, "f": 1, "o": 2, "g": 3}
    NG = len(GATES)
    GC = NG * R
    DMA = 16
    TRANSPOSE_STEP, XPART_STEP = 2, 3

    ctx = ExitStack()
    with ctx:
        def sb(name, shape):
            return ctx.enter_context(nc.sbuf_tensor(name, shape, f32))

        def ps(name, shape):
            return ctx.enter_context(nc.psum_tensor(name, shape, f32))

        def sem(name):
            return ctx.enter_context(nc.semaphore(name))

        wx_raw = sb("wx_raw", [128, M, NG * D])
        wh_raw = sb("wh_raw", [128, M, NG * D])
        wx = sb("wx", [128, M, Q, M, GC])
        wh = sb("wh", [128, M, Q, M, GC])
        bias_raw = sb("bias_raw", [128, NG, QD])
        bias_rows = sb("bias_rows", [128, M, GC])
        ident = sb("ident", [128, 128])
        h0_rows = sb("h0_rows", [128, QD])
        h0_units = sb("h0_units", [128, QD])
        x_next = sb("x_next", [128, QD])
        x_units = sb("x_units", [128, QD])
        x_here = sb("x_here", [128, QD])
        x_part = sb("x_part", [128, M, GC])
        acts = [sb(f"acts{m}", [128, GC + R]) for m in range(M)]
        prods = [sb(f"prods{m}", [128, 2 * R]) for m in range(M)]
        c_units = [sb(f"c_units{m}", [128, R]) for m in range(M)]
        o_units = [sb(f"o_units{m}", [128, R]) for m in range(M)]
        tanh_c = [sb(f"tanh_c{m}", [128, N]) for m in range(M)]
        h_units = sb("h_units", [128, M, STEPS, N])
        h_rows = sb("h_rows", [128, QD])
        y_rows = sb("y_rows", [128, QD])

        gates = [[ps(f"gates{b}{m}", [128, 512]) for m in range(M)] for b in range(2)]
        x_acc = [ps(f"x_acc{m}", [128, 512]) for m in range(M)]

        loaded_w = sem("loaded_w")
        loaded_small = sem("loaded_small")
        zeroed = sem("zeroed")
        ident_zeroed = sem("ident_zeroed")
        ident_made = sem("ident_made")
        weights_made = sem("weights_made")
        h0_turned = sem("h0_turned")
        x_next_loaded = sem("x_next_loaded")
        x_turned = sem("x_turned")
        x_here_loaded = sem("x_here_loaded")
        x_acc_done = sem("x_acc_done")
        x_part_made = sem("x_part_made")
        injected = sem("injected")
        h_turned_back = sem("h_turned_back")
        y_made = sem("y_made")
        y_stored = sem("y_stored")
        gates_done = [sem(f"gates_done{m}") for m in range(M)]
        acts_done = [sem(f"acts_done{m}") for m in range(M)]
        prods_done = [sem(f"prods_done{m}") for m in range(M)]
        c_done = [sem(f"c_done{m}") for m in range(M)]
        c_turned = [sem(f"c_turned{m}") for m in range(M)]
        tanh_done = [sem(f"tanh_done{m}") for m in range(M)]
        h_done = [sem(f"h_done{m}") for m in range(M)]

        block = ctx.enter_context(nc.Block())

        def x_quadrant(ap, t0, q):
            return ap[:, bass.ds(t0, STEPS), q * QD:(q + 1) * QD].rearrange("n t c -> t n c")

        @block.sync
        def _(sp):
            for q in range(Q):
                rows = slice(q * R, (q + 1) * R)
                sp.dma_start(x_next[rows, :], x_quadrant(x, 0, q)).then_inc(x_next_loaded, DMA)
            for m in range(M):
                for q in range(Q):
                    rows = slice(q * R, (q + 1) * R)
                    lines = slice(q * QD + m * R, q * QD + (m + 1) * R)
                    sp.dma_start(wx_raw[rows, m, :], w_x[lines, :]).then_inc(loaded_w, DMA)
            for m in range(M):
                for q in range(Q):
                    rows = slice(q * R, (q + 1) * R)
                    lines = slice(q * QD + m * R, q * QD + (m + 1) * R)
                    sp.dma_start(wh_raw[rows, m, :], w_h[lines, :]).then_inc(loaded_w, DMA)

            def load_here(t0):
                for q in range(Q):
                    sp.dma_start(x_here[q * R:(q + 1) * R, :], x_quadrant(x, t0, q)).then_inc(x_here_loaded, DMA)

            def store(t0, chunk):
                sp.wait_ge(y_made, chunk + 1)
                for q in range(Q):
                    sp.dma_start(x_quadrant(out, t0, q), y_rows[q * R:(q + 1) * R, :]).then_inc(y_stored, DMA)

            with sp.Fori(0, T // STEPS - 1) as k:
                sp.wait_ge(x_turned, k + 1)
                for q in range(Q):
                    sp.dma_start(x_next[q * R:(q + 1) * R, :],
                                 x_quadrant(x, (k + 1) * STEPS, q)).then_inc(x_next_loaded, DMA)
                load_here(k * STEPS)
                store(k * STEPS, k)
            load_here(T - STEPS)
            store(T - STEPS, T // STEPS - 1)
            sp.wait_ge(y_stored, T // STEPS * Q * DMA)

        @block.gpsimd
        def _(pool):
            nc.gpsimd.memset(ident[:], 0.0).then_inc(ident_zeroed, 1)
            pool.wait_ge(ident_zeroed, 1)
            nc.gpsimd.affine_select(out=ident[:], in_=ident[:], compare_op=ALU.not_equal, fill=1.0, base=0,
                                    pattern=[[-1, 128]], channel_multiplier=1).then_inc(ident_made, 1)

        @block.scalar
        def _(act):
            act.wait_ge(zeroed, 1)
            for q in range(Q):
                act.dma_start(h0_rows[q * R:q * R + N, :], cond[:, q * QD:(q + 1) * QD]).then_inc(loaded_small, DMA)
                act.dma_start(bias_raw[q * R:(q + 1) * R, :, :],
                              bias.rearrange("(g q c) -> q g c", g=NG, q=Q)[q:q + 1, :, :].broadcast_to(
                                  [R, NG, QD])).then_inc(loaded_small, DMA)
            with act.Fori(0, T, STEPS) as t0:
                for t in range(STEPS):
                    for m in range(M):
                        act.wait_ge(gates_done[m], t0 + (t + 1))
                        nc.scalar.activation(acts[m][:, 0:GC], gates[t % 2][m][:, 0:GC],
                                             ACT.Tanh).then_inc(acts_done[m], 1)
                    for m in range(M):
                        act.wait_ge(c_turned[m], t0 + (t + 1))
                        nc.scalar.activation(tanh_c[m][:], c_units[m][:, 0:N], ACT.Tanh,
                                             scale=0.5).then_inc(tanh_done[m], 1)

        @block.vector
        def _(dve):
            nc.vector.memset(h0_rows[:], 0.0).then_inc(zeroed, 1)
            for m in range(M):
                nc.vector.memset(acts[m][:], 0.0)
                for b in range(2):
                    last = nc.vector.memset(gates[b][m][:, 0:GC], 0.0)
            last.then_inc(zeroed, 1)
            dve.wait_ge(loaded_small, 2 * Q * DMA)
            nc.vector.transpose(h0_units[:], h0_rows[:]).then_inc(h0_turned, 1)
            dve.wait_ge(h0_turned, 1)
            for m in range(M):
                nc.vector.tensor_scalar(h_units[:, m, STEPS - 1, :], h0_units[:, m * R:m * R + N],
                                        2.0, None, ALU.mult).then_inc(h_done[m], 1)
            dve.wait_ge(x_next_loaded, Q * DMA)
            nc.vector.transpose(x_units[:], x_next[:]).then_inc(x_turned, 1)
            for g, gate in enumerate(GATES):
                half = 1.0 if gate == "g" else 0.5
                src = SOURCE[gate]
                nc.vector.tensor_scalar(bias_rows[:, :, g * R:(g + 1) * R],
                                        bias_raw[:, src, :].rearrange("p (m r) -> p m r", m=M),
                                        half, None, ALU.mult)
            dve.wait_ge(loaded_w, 4 * Q * DMA)
            for raw, made, factor in ((wx_raw, wx, 1.0), (wh_raw, wh, 0.5)):
                for b in range(M):
                    for g, gate in enumerate(GATES):
                        half = 1.0 if gate == "g" else 0.5
                        src = SOURCE[gate]
                        last = nc.vector.tensor_scalar(
                            made[:, b, :, :, g * R:(g + 1) * R],
                            raw[:, b, src * D:(src + 1) * D].rearrange("p (q m r) -> p q m r", q=Q, m=M),
                            half * factor, None, ALU.mult)
                last.then_inc(weights_made, 1)

            def make_x_part(chunk):
                for m in range(M):
                    dve.wait_ge(x_acc_done, (chunk + 1) * M)
                    nc.vector.tensor_tensor(x_part[:, m, :], x_acc[m][:, 0:GC], bias_rows[:, m, :],
                                            ALU.add).then_inc(x_part_made, 1)

            dve.wait_ge(weights_made, 2)
            make_x_part(0)

            def step(t0, t, chunk, ahead):
                now = t0 + (t + 1)
                if ahead and t == TRANSPOSE_STEP:
                    dve.wait_ge(x_next_loaded, (chunk + 2) * (Q * DMA))
                    nc.vector.transpose(x_units[:], x_next[:]).then_inc(x_turned, 1)
                if ahead and t == STEPS - 1:
                    dve.wait_ge(injected, now)
                    make_x_part(chunk + 1)

                def product(m):
                    dve.wait_ge(acts_done[m], now)
                    nc.vector.scalar_tensor_tensor(out=prods[m][:], in0=acts[m][:, R:3 * R], scalar=1.0,
                                                   in1=acts[m][:, 3 * R:5 * R], op0=ALU.add,
                                                   op1=ALU.mult).then_inc(prods_done[m], 1)

                def turn_o(m):
                    nc.vector.transpose(o_units[m][:], acts[m][:, 0:R])

                def cell(m):
                    dve.wait_ge(prods_done[m], now)
                    nc.vector.scalar_tensor_tensor(out=acts[m][:, GC:GC + R], in0=prods[m][:, R:2 * R], scalar=0.5,
                                                   in1=prods[m][:, 0:R], op0=ALU.mult,
                                                   op1=ALU.add).then_inc(c_done[m], 1)

                def turn_c(m):
                    dve.wait_ge(c_done[m], now)
                    nc.vector.transpose(c_units[m][:], acts[m][:, GC:GC + R]).then_inc(c_turned[m], 1)

                def hidden(m):
                    dve.wait_ge(tanh_done[m], now)
                    nc.vector.scalar_tensor_tensor(out=h_units[:, m, t, :], in0=o_units[m][:, 0:N], scalar=1.0,
                                                   in1=tanh_c[m][:], op0=ALU.add,
                                                   op1=ALU.mult).then_inc(h_done[m], 1)

                product(0)
                turn_o(0)
                cell(0)
                product(1)
                turn_c(0)
                turn_o(1)
                cell(1)
                turn_c(1)
                hidden(0)
                hidden(1)

            def residual(t0, chunk):
                for m in range(M):
                    dve.wait_ge(h_done[m], t0 + (STEPS + 1))
                nc.vector.transpose(h_rows[:], h_units[:].rearrange("p m t n -> p (m t n)")).then_inc(h_turned_back, 1)
                dve.wait_ge(h_turned_back, chunk + 1)
                dve.wait_ge(x_here_loaded, (chunk + 1) * (Q * DMA))
                dve.wait_ge(y_stored, chunk * (Q * DMA))
                nc.vector.scalar_tensor_tensor(out=y_rows[:], in0=h_rows[:], scalar=0.5, in1=x_here[:],
                                               op0=ALU.mult, op1=ALU.add).then_inc(y_made, 1)

            with dve.Fori(0, T // STEPS - 1) as k:
                for t in range(STEPS):
                    step(k * STEPS, t, k, True)
                residual(k * STEPS, k)
            for t in range(STEPS):
                step(T - STEPS, t, T // STEPS - 1, False)
            residual(T - STEPS, T // STEPS - 1)

        @block.tensor
        def _(pe):
            def x_product(m, b, chunk):
                if m == 0 and b == 0:
                    pe.wait_ge(x_turned, chunk + 1)
                for q in range(Q):
                    last = nc.tensor.matmul(x_acc[m][q * R:(q + 1) * R, 0:GC], x_units[:, b * R:(b + 1) * R],
                                            wx[:, b, q, m, :], start=b == 0, stop=b == M - 1,
                                            tile_position=(0, q * R))
                if b == M - 1:
                    last.then_inc(x_acc_done, 1)

            def inject(t):
                for m in range(M):
                    for q in range(Q):
                        at = q * R + t * N
                        last = nc.tensor.matmul(gates[t % 2][m][q * R:q * R + N, 0:GC], ident[:, at:at + N],
                                                x_part[:, m, :], start=True, stop=False, tile_position=(0, q * R))
                last.then_inc(injected, 1)

            def step(t0, t, chunk, ahead):
                now = t0 + (t + 1)
                before = (t - 1) % STEPS
                for b in range(M):
                    pe.wait_ge(h_done[b], now)
                    for m in range(M):
                        for q in range(Q):
                            last = nc.tensor.matmul(gates[t % 2][m][q * R:q * R + N, 0:GC], h_units[:, b, before, :],
                                                    wh[:, b, q, m, :], start=False, stop=b == M - 1,
                                                    tile_position=(0, q * R))
                        if b == M - 1:
                            last.then_inc(gates_done[m], 1)
                if t < STEPS - 1:
                    inject(t + 1)
                elif ahead:
                    pe.wait_ge(x_part_made, (chunk + 2) * M)
                    inject(0)
                if ahead and XPART_STEP <= t < XPART_STEP + M * M:
                    x_product((t - XPART_STEP) // M, (t - XPART_STEP) % M, chunk + 1)

            pe.wait_ge(weights_made, 2)
            pe.wait_ge(zeroed, 2)
            for m in range(M):
                for b in range(M):
                    x_product(m, b, 0)
            pe.wait_ge(ident_made, 1)
            pe.wait_ge(x_part_made, M)
            inject(0)
            with pe.Fori(0, T // STEPS - 1) as k:
                for t in range(STEPS):
                    step(k * STEPS, t, k, True)
            for t in range(STEPS):
                step(T - STEPS, t, T // STEPS - 1, False)


_INS = ['x', 'cond_1024', 'L0_cond_Wx', 'L0_cond_Wh', 'L0_cond_b']


def kernel(**inputs):
    import numpy as _np
    import concourse.bacc as _bacc
    from concourse import mybir as _mybir
    from concourse.bass_utils import run_bass_kernel_spmd as _run

    nc = _bacc.Bacc("TRN2", target_bir_lowering=False, num_devices=1)
    arrays, args = {}, []
    for name in _INS:
        a = _np.ascontiguousarray(inputs[name])
        arrays[f"in_{name}_dram"] = a
        args.append(nc.dram_tensor(f"in_{name}_dram", a.shape, _mybir.dt.from_np(a.dtype), kind="ExternalInput").ap())
    shape = inputs["x"].shape
    args.append(nc.dram_tensor("out_dram", shape, _mybir.dt.float32, kind="ExternalOutput").ap())
    lstm_residual_kernel(nc, *args)
    r = _run(nc, [arrays], core_ids=[0])
    return r.results[0]["out_dram"]
```

```python
import concourse.bass as bass
from concourse import mybir
from contextlib import ExitStack


def lstm_residual_kernel(nc: bass.Bass, x: bass.AP, cond: bass.AP, w_x: bass.AP, w_h: bass.AP, bias: bass.AP,
                         out: bass.AP):
    f32 = mybir.dt.float32
    ACT = mybir.ActivationFunctionType
    ALU = mybir.AluOpType

    N, T, D = x.shape
    Q, M, R = 4, 2, 32
    QD = M * R
    STEPS = R // N
    GATES = ("o", "i", "f", "g")
    SOURCE = {"i": 0, "f": 1, "o": 2, "g": 3}
    NG = len(GATES)
    GC = NG * R
    CHUNKS = T // STEPS
    DMA = 16
    PAIRS = 2
    PIECES = [(m, b, p) for m in range(M) for b in range(M) for p in range(PAIRS)]
    PIECES_AT = [[], [], PIECES[0:2], PIECES[2:4], PIECES[4:6], PIECES[6:7], PIECES[7:8], []]

    ctx = ExitStack()
    with ctx:
        def sb(name, shape):
            return ctx.enter_context(nc.sbuf_tensor(name, shape, f32))

        def ps(name, shape):
            return ctx.enter_context(nc.psum_tensor(name, shape, f32))

        def sem(name):
            return ctx.enter_context(nc.semaphore(name))

        wx_raw = sb("wx_raw", [128, M, NG * D])
        wh_raw = sb("wh_raw", [128, M, NG * D])
        wx = sb("wx", [128, M, Q, M, GC])
        wh = sb("wh", [128, M, Q, M, GC])
        bias_raw = sb("bias_raw", [128, NG, QD])
        bias_rows = sb("bias_rows", [128, M, GC])
        ident = sb("ident", [128, 128])
        h0_rows = sb("h0_rows", [128, QD])
        table_probe = sb("table_probe", [128, 2])
        h0_units = sb("h0_units", [128, QD])
        x_next = sb("x_next", [128, QD])
        x_units = sb("x_units", [128, QD])
        x_here = sb("x_here", [128, QD])
        x_part = sb("x_part", [128, M, GC])
        acts = [sb(f"acts{m}", [128, NG + 1, N]) for m in range(M)]
        prods = [sb(f"prods{m}", [128, 2, N]) for m in range(M)]
        h_units = sb("h_units", [128, M, STEPS, N])
        h_rows = sb("h_rows", [128, QD])
        y_rows = sb("y_rows", [128, QD])

        gates = [[ps(f"gates{b}{m}", [128, 512]) for m in range(M)] for b in range(2)]
        x_acc = [ps(f"x_acc{m}", [128, 512]) for m in range(M)]
        cell_bank = [ps(f"cell_bank{m}", [128, 512]) for m in range(M)]
        turned = [cell_bank[m][:, 0:GC] for m in range(M)]
        tanh_c = [cell_bank[m][:, GC:GC + N] for m in range(M)]

        loaded_w = sem("loaded_w")
        loaded_small = sem("loaded_small")
        zeroed = sem("zeroed")
        ident_zeroed = sem("ident_zeroed")
        ident_made = sem("ident_made")
        weights_made = sem("weights_made")
        h0_turned = sem("h0_turned")
        x_next_loaded = sem("x_next_loaded")
        x_turned = sem("x_turned")
        x_here_loaded = sem("x_here_loaded")
        x_acc_done = sem("x_acc_done")
        x_part_made = sem("x_part_made")
        injected = sem("injected")
        h_turned_back = sem("h_turned_back")
        y_made = sem("y_made")
        y_stored = sem("y_stored")
        gates_done = [sem(f"gates_done{m}") for m in range(M)]
        gates_turned = [sem(f"gates_turned{m}") for m in range(M)]
        acts_done = [sem(f"acts_done{m}") for m in range(M)]
        prods_done = [sem(f"prods_done{m}") for m in range(M)]
        c_done = [sem(f"c_done{m}") for m in range(M)]
        tanh_done = [sem(f"tanh_done{m}") for m in range(M)]
        h_done = [sem(f"h_done{m}") for m in range(M)]

        block = ctx.enter_context(nc.Block())

        def x_quadrant(ap, t0, q):
            return ap[:, bass.ds(t0, STEPS), q * QD:(q + 1) * QD].rearrange("n t c -> t n c")

        @block.sync
        def _(sp):
            for q in range(Q):
                rows = slice(q * R, (q + 1) * R)
                sp.dma_start(x_next[rows, :], x_quadrant(x, 0, q)).then_inc(x_next_loaded, DMA)
            for m in range(M):
                for q in range(Q):
                    rows = slice(q * R, (q + 1) * R)
                    lines = slice(q * QD + m * R, q * QD + (m + 1) * R)
                    sp.dma_start(wx_raw[rows, m, :], w_x[lines, :]).then_inc(loaded_w, DMA)
            for m in range(M):
                for q in range(Q):
                    rows = slice(q * R, (q + 1) * R)
                    lines = slice(q * QD + m * R, q * QD + (m + 1) * R)
                    sp.dma_start(wh_raw[rows, m, :], w_h[lines, :]).then_inc(loaded_w, DMA)

            def load_next(chunk):
                sp.wait_ge(x_turned, chunk)
                for q in range(Q):
                    sp.dma_start(x_next[q * R:(q + 1) * R, :],
                                 x_quadrant(x, chunk * STEPS, q)).then_inc(x_next_loaded, DMA)

            def load_here(chunk):
                for q in range(Q):
                    sp.dma_start(x_here[q * R:(q + 1) * R, :],
                                 x_quadrant(x, chunk * STEPS, q)).then_inc(x_here_loaded, DMA)

            def store(chunk):
                sp.wait_ge(y_made, chunk + 1)
                for q in range(Q):
                    sp.dma_start(x_quadrant(out, chunk * STEPS, q),
                                 y_rows[q * R:(q + 1) * R, :]).then_inc(y_stored, DMA)
                sp.wait_ge(y_stored, (chunk + 1) * (Q * DMA))

            load_next(1)
            load_here(0)
            with sp.Fori(0, CHUNKS - 2) as k:
                load_next(k + 2)
                store(k)
                load_here(k + 1)
            store(CHUNKS - 2)
            load_here(CHUNKS - 1)
            store(CHUNKS - 1)

        @block.gpsimd
        def _(pool):
            nc.gpsimd.memset(ident[:], 0.0).then_inc(ident_zeroed, 1)
            pool.wait_ge(ident_zeroed, 1)
            nc.gpsimd.affine_select(out=ident[:], in_=ident[:], compare_op=ALU.not_equal, fill=1.0, base=0,
                                    pattern=[[-1, 128]], channel_multiplier=1).then_inc(ident_made, 1)

        @block.scalar
        def _(act):
            act.wait_ge(zeroed, 1)
            for q in range(Q):
                act.dma_start(h0_rows[q * R:q * R + N, :], cond[:, q * QD:(q + 1) * QD]).then_inc(loaded_small, DMA)
                act.dma_start(bias_raw[q * R:(q + 1) * R, :, :],
                              bias.rearrange("(g q c) -> q g c", g=NG, q=Q)[q:q + 1, :, :].broadcast_to(
                                  [R, NG, QD])).then_inc(loaded_small, DMA)
            nc.scalar.activation(table_probe[:, 1:2], table_probe[:, 0:1], ACT.Tanh)
            with act.Fori(0, T, STEPS) as t0:
                for t in range(STEPS):
                    for m in range(M):
                        act.wait_ge(gates_turned[m], t0 + (t + 1))
                        nc.scalar.activation(acts[m][:, 0:NG, :],
                                             turned[m].rearrange("p (g c) -> p g c", g=NG)[:, :, 0:N],
                                             ACT.Tanh).then_inc(acts_done[m], 1)
                    for m in range(M):
                        act.wait_ge(c_done[m], t0 + (t + 1))
                        nc.scalar.activation(tanh_c[m], acts[m][:, NG, :], ACT.Tanh,
                                             scale=0.5).then_inc(tanh_done[m], 1)

        @block.vector
        def _(dve):
            nc.vector.memset(table_probe[:], 0.0)
            nc.vector.memset(h0_rows[:], 0.0).then_inc(zeroed, 1)
            for m in range(M):
                nc.vector.memset(acts[m][:], 0.0)
                for b in range(2):
                    last = nc.vector.memset(gates[b][m][:, 0:GC], 0.0)
            last.then_inc(zeroed, 1)
            dve.wait_ge(loaded_small, 2 * Q * DMA)
            nc.vector.transpose(h0_units[:], h0_rows[:]).then_inc(h0_turned, 1)
            dve.wait_ge(h0_turned, 1)
            for m in range(M):
                nc.vector.tensor_scalar(h_units[:, m, STEPS - 1, :], h0_units[:, m * R:m * R + N],
                                        2.0, None, ALU.mult).then_inc(h_done[m], 1)
            dve.wait_ge(x_next_loaded, Q * DMA)
            nc.vector.transpose(x_units[:], x_next[:]).then_inc(x_turned, 1)
            for g, gate in enumerate(GATES):
                half = 1.0 if gate == "g" else 0.5
                src = SOURCE[gate]
                nc.vector.tensor_scalar(bias_rows[:, :, g * R:(g + 1) * R],
                                        bias_raw[:, src, :].rearrange("p (m r) -> p m r", m=M),
                                        half, None, ALU.mult)
            dve.wait_ge(loaded_w, 4 * Q * DMA)
            for raw, made, factor in ((wx_raw, wx, 1.0), (wh_raw, wh, 0.5)):
                for b in range(M):
                    for g, gate in enumerate(GATES):
                        half = 1.0 if gate == "g" else 0.5
                        src = SOURCE[gate]
                        last = nc.vector.tensor_scalar(
                            made[:, b, :, :, g * R:(g + 1) * R],
                            raw[:, b, src * D:(src + 1) * D].rearrange("p (q m r) -> p q m r", q=Q, m=M),
                            half * factor, None, ALU.mult)
                last.then_inc(weights_made, 1)

            def make_x_part(chunk):
                for m in range(M):
                    dve.wait_ge(x_acc_done, (chunk + 1) * M)
                    nc.vector.tensor_tensor(x_part[:, m, :], x_acc[m][:, 0:GC], bias_rows[:, m, :],
                                            ALU.add).then_inc(x_part_made, 1)

            dve.wait_ge(weights_made, 2)
            make_x_part(0)

            def turn_back(chunk):
                for m in range(M):
                    dve.wait_ge(h_done[m], chunk * STEPS + (STEPS + 1))
                nc.vector.transpose(h_rows[:], h_units[:].rearrange("p m t n -> p (m t n)")).then_inc(h_turned_back, 1)

            def residual(chunk):
                dve.wait_ge(h_turned_back, chunk + 1)
                dve.wait_ge(x_here_loaded, (chunk + 1) * (Q * DMA))
                nc.vector.scalar_tensor_tensor(out=y_rows[:], in0=h_rows[:], scalar=0.5, in1=x_here[:],
                                               op0=ALU.mult, op1=ALU.add).then_inc(y_made, 1)

            def step(chunk, t, first, ahead):
                now = chunk * STEPS + (t + 1)
                if not first and t == 0:
                    turn_back(chunk - 1)
                if not first and t == 1:
                    residual(chunk - 1)
                if ahead and t == 2:
                    dve.wait_ge(x_next_loaded, (chunk + 2) * (Q * DMA))
                    nc.vector.transpose(x_units[:], x_next[:]).then_inc(x_turned, 1)
                if ahead and t == STEPS - 1:
                    dve.wait_ge(injected, now)
                    make_x_part(chunk + 1)

                def turn(m):
                    dve.wait_ge(gates_done[m], now)
                    nc.vector.transpose(turned[m], gates[t % 2][m][:, 0:GC]).then_inc(gates_turned[m], 1)

                def product(m):
                    dve.wait_ge(acts_done[m], now)
                    nc.vector.scalar_tensor_tensor(out=prods[m][:], in0=acts[m][:, 1:3, :], scalar=1.0,
                                                   in1=acts[m][:, 3:5, :], op0=ALU.add,
                                                   op1=ALU.mult).then_inc(prods_done[m], 1)

                def cell(m):
                    dve.wait_ge(prods_done[m], now)
                    nc.vector.scalar_tensor_tensor(out=acts[m][:, NG, :], in0=prods[m][:, 1, :], scalar=0.5,
                                                   in1=prods[m][:, 0, :], op0=ALU.mult,
                                                   op1=ALU.add).then_inc(c_done[m], 1)

                def hidden(m):
                    dve.wait_ge(tanh_done[m], now)
                    nc.vector.scalar_tensor_tensor(out=h_units[:, m, t, :], in0=acts[m][:, 0, :], scalar=1.0,
                                                   in1=tanh_c[m], op0=ALU.add,
                                                   op1=ALU.mult).then_inc(h_done[m], 1)

                turn(0)
                turn(1)
                product(0)
                cell(0)
                product(1)
                cell(1)
                hidden(0)
                hidden(1)

            for t in range(STEPS):
                step(0, t, True, True)
            with dve.Fori(1, CHUNKS - 1) as k:
                for t in range(STEPS):
                    step(k, t, False, True)
            for t in range(STEPS):
                step(CHUNKS - 1, t, False, False)
            turn_back(CHUNKS - 1)
            residual(CHUNKS - 1)

        @block.tensor
        def _(pe):
            def x_product(m, b, pair, chunk):
                if (m, b, pair) == PIECES[0]:
                    pe.wait_ge(x_turned, chunk + 1)
                for q in range(pair * Q // PAIRS, (pair + 1) * Q // PAIRS):
                    last = nc.tensor.matmul(x_acc[m][q * R:(q + 1) * R, 0:GC], x_units[:, b * R:(b + 1) * R],
                                            wx[:, b, q, m, :], start=b == 0, stop=b == M - 1,
                                            tile_position=(0, q * R))
                if b == M - 1 and pair == PAIRS - 1:
                    last.then_inc(x_acc_done, 1)

            def inject(t):
                for m in range(M):
                    for q in range(Q):
                        at = q * R + t * N
                        last = nc.tensor.matmul(gates[t % 2][m][q * R:q * R + N, 0:GC], ident[:, at:at + N],
                                                x_part[:, m, :], start=True, stop=False, tile_position=(0, q * R))
                last.then_inc(injected, 1)

            def step(t0, t, chunk, ahead):
                now = t0 + (t + 1)
                before = (t - 1) % STEPS
                for b in range(M):
                    pe.wait_ge(h_done[b], now)
                    for m in range(M):
                        for q in range(Q):
                            last = nc.tensor.matmul(gates[t % 2][m][q * R:q * R + N, 0:GC], h_units[:, b, before, :],
                                                    wh[:, b, q, m, :], start=False, stop=b == M - 1,
                                                    tile_position=(0, q * R))
                        if b == M - 1:
                            last.then_inc(gates_done[m], 1)
                if t < STEPS - 1:
                    inject(t + 1)
                elif ahead:
                    pe.wait_ge(x_part_made, (chunk + 2) * M)
                    inject(0)
                if ahead:
                    for piece in PIECES_AT[t]:
                        x_product(*piece, chunk + 1)

            pe.wait_ge(weights_made, 2)
            pe.wait_ge(zeroed, 2)
            for piece in PIECES:
                x_product(*piece, 0)
            pe.wait_ge(ident_made, 1)
            pe.wait_ge(x_part_made, M)
            inject(0)
            with pe.Fori(0, CHUNKS - 1) as k:
                for t in range(STEPS):
                    step(k * STEPS, t, k, True)
            for t in range(STEPS):
                step(T - STEPS, t, CHUNKS - 1, False)


_INS = ['x', 'cond_1024', 'L0_cond_Wx', 'L0_cond_Wh', 'L0_cond_b']


def kernel(**inputs):
    import numpy as _np
    import concourse.bacc as _bacc
    from concourse import mybir as _mybir
    from concourse.bass_utils import run_bass_kernel_spmd as _run

    nc = _bacc.Bacc("TRN2", target_bir_lowering=False, num_devices=1)
    arrays, args = {}, []
    for name in _INS:
        a = _np.ascontiguousarray(inputs[name])
        arrays[f"in_{name}_dram"] = a
        args.append(nc.dram_tensor(f"in_{name}_dram", a.shape, _mybir.dt.from_np(a.dtype), kind="ExternalInput").ap())
    shape = inputs["x"].shape
    args.append(nc.dram_tensor("out_dram", shape, _mybir.dt.float32, kind="ExternalOutput").ap())
    lstm_residual_kernel(nc, *args)
    r = _run(nc, [arrays], core_ids=[0])
    return r.results[0]["out_dram"]
```

```python
import concourse.bass as bass
from concourse import mybir
from contextlib import ExitStack


def lstm_residual_kernel(nc: bass.Bass, x: bass.AP, cond: bass.AP, w_x: bass.AP, w_h: bass.AP, bias: bass.AP,
                         out: bass.AP):
    f32 = mybir.dt.float32
    ACT = mybir.ActivationFunctionType
    ALU = mybir.AluOpType

    N, T, D = x.shape
    Q, M, R = 4, 2, 32
    QD = M * R
    STEPS = R // N
    I, F, O, G = range(4)
    NG = w_h.shape[1] // D
    IFG = (I, F, G)
    IC, OC = len(IFG) * R, M * R
    GC = M * IC + OC
    O_COLUMNS = slice(M * IC, GC)
    TURNS = 2
    CHUNKS = T // STEPS
    DMA = 16
    PIECES = [(b, slice(c * GC // 2, (c + 1) * GC // 2)) for b in range(M) for c in range(2)]
    FIRST_PIECE_AT = 2

    ctx = ExitStack()
    with ctx:
        def sb(name, shape):
            return ctx.enter_context(nc.sbuf_tensor(name, shape, f32))

        def ps(name, shape):
            return ctx.enter_context(nc.psum_tensor(name, shape, f32))

        def sem(name):
            return ctx.enter_context(nc.semaphore(name))

        wx_raw = sb("wx_raw", [128, M, NG * D])
        wh_raw = sb("wh_raw", [128, M, NG * D])
        wx = sb("wx", [128, M, Q, GC])
        wh = sb("wh", [128, M, Q, GC])
        bias_raw = sb("bias_raw", [128, NG, QD])
        bias_rows = sb("bias_rows", [128, GC])
        ident = sb("ident", [128, 128])
        h0_rows = sb("h0_rows", [128, QD])
        table_probe = sb("table_probe", [128, 2])
        h0_units = sb("h0_units", [128, QD])
        x_next = sb("x_next", [128, QD])
        x_units = sb("x_units", [128, QD])
        x_here = sb("x_here", [128, QD])
        x_part = sb("x_part", [128, GC])
        acts = [sb(f"acts{m}", [128, len(IFG) + 1, N]) for m in range(M)]
        tanh_o = sb("tanh_o", [128, M, N])
        prods = [sb(f"prods{m}", [128, 2, N]) for m in range(M)]
        h_units = sb("h_units", [128, M, STEPS, N])
        h_rows = sb("h_rows", [128, QD])
        y_rows = sb("y_rows", [128, QD])

        gates = [[ps(f"gates{b}{m}", [128, 512]) for m in range(M)] for b in range(TURNS)]
        gates_o = ps("gates_o", [128, 512])
        x_acc = ps("x_acc", [128, 512])
        cell_bank = [ps(f"cell_bank{m}", [128, 512]) for m in range(M)]
        turned = [cell_bank[m][:, 0:IC] for m in range(M)]
        tanh_c = [cell_bank[m][:, IC:IC + N] for m in range(M)]
        o_turned = cell_bank[0][:, GC // 2:GC // 2 + OC]

        wx_loaded = [sem(f"wx_loaded{b}") for b in range(M)]
        wh_loaded = [sem(f"wh_loaded{b}") for b in range(M)]
        bias_loaded = sem("bias_loaded")
        h0_loaded = sem("h0_loaded")
        zeroed = sem("zeroed")
        ident_zeroed = sem("ident_zeroed")
        ident_made = sem("ident_made")
        wx_made = sem("wx_made")
        wh_made = sem("wh_made")
        bias_made = sem("bias_made")
        h0_turned = sem("h0_turned")
        x_next_loaded = sem("x_next_loaded")
        x_turned = sem("x_turned")
        x_here_loaded = sem("x_here_loaded")
        x_acc_done = sem("x_acc_done")
        x_part_made = sem("x_part_made")
        h_turned_back = sem("h_turned_back")
        y_made = sem("y_made")
        y_stored = sem("y_stored")
        injected = sem("injected")
        gates_o_done = sem("gates_o_done")
        o_turn_done = sem("o_turn_done")
        gates_done = [sem(f"gates_done{m}") for m in range(M)]
        gates_turned = [sem(f"gates_turned{m}") for m in range(M)]
        acts_done = [sem(f"acts_done{m}") for m in range(M)]
        prods_done = [sem(f"prods_done{m}") for m in range(M)]
        c_done = [sem(f"c_done{m}") for m in range(M)]
        tanh_done = [sem(f"tanh_done{m}") for m in range(M)]
        h_done = [sem(f"h_done{m}") for m in range(M)]

        block = ctx.enter_context(nc.Block())

        def x_quadrant(ap, t0, q):
            return ap[:, bass.ds(t0, STEPS), q * QD:(q + 1) * QD].rearrange("n t c -> t n c")

        @block.sync
        def _(sp):
            def load_weights(raw, w, loaded):
                for b in range(M):
                    sp.dma_start(raw[:, b, :],
                                 w.rearrange("(q b r) c -> b q r c", q=Q, b=M)[b]).then_inc(loaded[b], DMA)

            load_weights(wx_raw, w_x, wx_loaded)
            for q in range(Q):
                sp.dma_start(x_next[q * R:(q + 1) * R, :], x_quadrant(x, 0, q)).then_inc(x_next_loaded, DMA)
            load_weights(wh_raw, w_h, wh_loaded)

            def load_next(chunk):
                sp.wait_ge(x_turned, chunk)
                for q in range(Q):
                    sp.dma_start(x_next[q * R:(q + 1) * R, :],
                                 x_quadrant(x, chunk * STEPS, q)).then_inc(x_next_loaded, DMA)

            def load_here(chunk):
                for q in range(Q):
                    sp.dma_start(x_here[q * R:(q + 1) * R, :],
                                 x_quadrant(x, chunk * STEPS, q)).then_inc(x_here_loaded, DMA)

            def store(chunk):
                sp.wait_ge(y_made, chunk + 1)
                for q in range(Q):
                    sp.dma_start(x_quadrant(out, chunk * STEPS, q),
                                 y_rows[q * R:(q + 1) * R, :]).then_inc(y_stored, DMA)
                sp.wait_ge(y_stored, (chunk + 1) * (Q * DMA))

            load_next(1)
            load_here(0)
            with sp.Fori(0, CHUNKS - 2) as k:
                load_next(k + 2)
                store(k)
                load_here(k + 1)
            store(CHUNKS - 2)
            load_here(CHUNKS - 1)
            store(CHUNKS - 1)

        @block.gpsimd
        def _(pool):
            nc.gpsimd.memset(ident[:], 0.0).then_inc(ident_zeroed, 1)
            pool.wait_ge(ident_zeroed, 1)
            nc.gpsimd.affine_select(out=ident[:], in_=ident[:], compare_op=ALU.not_equal, fill=1.0, base=0,
                                    pattern=[[-1, 128]], channel_multiplier=1).then_inc(ident_made, 1)

        @block.scalar
        def _(act):
            for q in range(Q):
                act.dma_start(bias_raw[q * R:(q + 1) * R, :, :],
                              bias.rearrange("(g q c) -> q g c", g=NG, q=Q)[q:q + 1, :, :].broadcast_to(
                                  [R, NG, QD])).then_inc(bias_loaded, DMA)
            act.wait_ge(zeroed, 1)
            for q in range(Q):
                act.dma_start(h0_rows[q * R:q * R + N, :], cond[:, q * QD:(q + 1) * QD]).then_inc(h0_loaded, DMA)
            nc.scalar.activation(table_probe[:, 1:2], table_probe[:, 0:1], ACT.Tanh)
            with act.Fori(0, T, STEPS) as t0:
                for t in range(STEPS):
                    for m in range(M):
                        act.wait_ge(gates_turned[m], t0 + (t + 1))
                        nc.scalar.activation(acts[m][:, 0:len(IFG), :],
                                             turned[m].rearrange("p (g c) -> p g c", g=len(IFG))[:, :, 0:N],
                                             ACT.Tanh).then_inc(acts_done[m], 1)
                    act.wait_ge(o_turn_done, t0 + (t + 1))
                    nc.scalar.activation(tanh_o[:], o_turned.rearrange("p (m c) -> p m c", m=M)[:, :, 0:N],
                                         ACT.Tanh)
                    for m in range(M):
                        act.wait_ge(c_done[m], t0 + (t + 1))
                        nc.scalar.activation(tanh_c[m], acts[m][:, len(IFG), :], ACT.Tanh,
                                             scale=0.5).then_inc(tanh_done[m], 1)

        @block.vector
        def _(dve):
            def permute(made, raw, factor):
                for g, gate in enumerate(IFG):
                    half = 1.0 if gate == G else 0.5
                    nc.vector.tensor_scalar(
                        made[:, :, 0:M * IC].rearrange("p q (m c) -> p q m c", m=M)[:, :, :, g * R:(g + 1) * R],
                        raw[:, gate, :, :].rearrange("p q (m r) -> p q m r", m=M), half * factor, None, ALU.mult)
                return nc.vector.tensor_scalar(made[:, :, O_COLUMNS], raw[:, O, :, :], 0.5 * factor, None, ALU.mult)

            def permute_matrix(made, raw, b, factor, loaded):
                dve.wait_ge(loaded[b], DMA)
                return permute(made[:, b, :, :], raw[:, b, :].rearrange("p (g q c) -> p g q c", g=NG, q=Q), factor)

            def make_x_part(chunk):
                dve.wait_ge(x_acc_done, chunk + 1)
                nc.vector.tensor_tensor(x_part[:], x_acc[:, 0:GC], bias_rows[:], ALU.add).then_inc(x_part_made, 1)

            nc.vector.memset(table_probe[:], 0.0)
            nc.vector.memset(h0_rows[:], 0.0).then_inc(zeroed, 1)
            for m in range(M):
                nc.vector.memset(acts[m][:], 0.0)
                for b in range(TURNS):
                    nc.vector.memset(gates[b][m][:, 0:IC], 0.0)
            nc.vector.memset(gates_o[:, 0:OC], 0.0).then_inc(zeroed, 1)

            for b in range(M):
                permute_matrix(wx, wx_raw, b, 1.0, wx_loaded).then_inc(wx_made, 1)
            dve.wait_ge(x_next_loaded, Q * DMA)
            nc.vector.transpose(x_units[:], x_next[:]).then_inc(x_turned, 1)
            dve.wait_ge(bias_loaded, Q * DMA)
            permute(bias_rows[:].rearrange("p (q c) -> p q c", q=1),
                    bias_raw[:].rearrange("p g (q c) -> p g q c", q=1), 1.0).then_inc(bias_made, 1)
            permute_matrix(wh, wh_raw, 0, 0.5, wh_loaded).then_inc(wh_made, 1)
            dve.wait_ge(bias_made, 1)
            make_x_part(0)
            permute_matrix(wh, wh_raw, 1, 0.5, wh_loaded).then_inc(wh_made, 1)
            dve.wait_ge(h0_loaded, Q * DMA)
            nc.vector.transpose(h0_units[:], h0_rows[:]).then_inc(h0_turned, 1)
            dve.wait_ge(h0_turned, 1)
            for m in range(M):
                nc.vector.tensor_scalar(h_units[:, m, STEPS - 1, :], h0_units[:, m * R:m * R + N],
                                        2.0, None, ALU.mult).then_inc(h_done[m], 1)

            def turn_back(chunk):
                for m in range(M):
                    dve.wait_ge(h_done[m], chunk * STEPS + (STEPS + 1))
                nc.vector.transpose(h_rows[:], h_units[:].rearrange("p m t n -> p (m t n)")).then_inc(h_turned_back, 1)

            def residual(chunk):
                dve.wait_ge(h_turned_back, chunk + 1)
                dve.wait_ge(x_here_loaded, (chunk + 1) * (Q * DMA))
                nc.vector.scalar_tensor_tensor(out=y_rows[:], in0=h_rows[:], scalar=0.5, in1=x_here[:],
                                               op0=ALU.mult, op1=ALU.add).then_inc(y_made, 1)

            def step(chunk, t, first, ahead):
                now = chunk * STEPS + (t + 1)
                if not first and t == 1:
                    residual(chunk - 1)
                if ahead and t == 2:
                    dve.wait_ge(x_next_loaded, (chunk + 2) * (Q * DMA))
                    nc.vector.transpose(x_units[:], x_next[:]).then_inc(x_turned, 1)
                if ahead and t == STEPS - 1:
                    dve.wait_ge(injected, now)
                    make_x_part(chunk + 1)

                def turn(m):
                    dve.wait_ge(gates_done[m], now)
                    nc.vector.transpose(turned[m], gates[t % TURNS][m][:, 0:IC]).then_inc(gates_turned[m], 1)

                def product(m):
                    dve.wait_ge(acts_done[m], now)
                    nc.vector.scalar_tensor_tensor(out=prods[m][:], in0=acts[m][:, 0:2, :], scalar=1.0,
                                                   in1=acts[m][:, 2:4, :], op0=ALU.add,
                                                   op1=ALU.mult).then_inc(prods_done[m], 1)

                def cell(m):
                    dve.wait_ge(prods_done[m], now)
                    nc.vector.scalar_tensor_tensor(out=acts[m][:, len(IFG), :], in0=prods[m][:, 1, :], scalar=0.5,
                                                   in1=prods[m][:, 0, :], op0=ALU.mult,
                                                   op1=ALU.add).then_inc(c_done[m], 1)

                def turn_o():
                    dve.wait_ge(gates_o_done, now)
                    nc.vector.transpose(o_turned, gates_o[:, 0:OC]).then_inc(o_turn_done, 1)

                def hidden(m):
                    dve.wait_ge(tanh_done[m], now)
                    nc.vector.scalar_tensor_tensor(out=h_units[:, m, t, :], in0=tanh_o[:, m, :], scalar=1.0,
                                                   in1=tanh_c[m], op0=ALU.add,
                                                   op1=ALU.mult).then_inc(h_done[m], 1)

                turn(0)
                if not first and t == 0:
                    turn_back(chunk - 1)
                turn(1)
                product(0)
                turn_o()
                cell(0)
                product(1)
                cell(1)
                hidden(0)
                hidden(1)

            for t in range(STEPS):
                step(0, t, True, True)
            with dve.Fori(1, CHUNKS - 1) as k:
                for t in range(STEPS):
                    step(k, t, False, True)
            for t in range(STEPS):
                step(CHUNKS - 1, t, False, False)
            turn_back(CHUNKS - 1)
            residual(CHUNKS - 1)

        @block.tensor
        def _(pe):
            def x_product(b, columns, chunk):
                opens = (b, columns) == PIECES[0]
                if opens:
                    pe.wait_ge(x_turned, chunk + 1)
                for q in range(Q):
                    last = nc.tensor.matmul(x_acc[q * R:(q + 1) * R, columns], x_units[:, b * R:(b + 1) * R],
                                            wx[:, b, q, columns], start=opens, stop=b == M - 1,
                                            tile_position=(0, q * R), skip_group_check=True)
                if (b, columns) == PIECES[-1]:
                    last.then_inc(x_acc_done, 1)

            def targets(t):
                return [(gates[t % TURNS][m], slice(m * IC, (m + 1) * IC)) for m in range(M)] + [(gates_o, O_COLUMNS)]

            def inject(t, before=None):
                for bank, columns in targets(t):
                    if bank is gates_o and before is not None:
                        pe.wait_ge(o_turn_done, before)
                    for q in range(Q):
                        at = q * R + t * N
                        last = nc.tensor.matmul(bank[q * R:q * R + N, 0:columns.stop - columns.start],
                                                ident[:, at:at + N], x_part[:, columns], start=True, stop=False,
                                                tile_position=(0, q * R))
                last.then_inc(injected, 1)

            def step(chunk, t, ahead):
                now = chunk * STEPS + (t + 1)
                first, second, both_o = targets(t)

                def recur(b, target):
                    bank, columns = target
                    for q in range(Q):
                        last = nc.tensor.matmul(bank[q * R:q * R + N, 0:columns.stop - columns.start],
                                                h_units[:, b, (t - 1) % STEPS, :], wh[:, b, q, columns],
                                                start=False, stop=b == M - 1, tile_position=(0, q * R))
                    return last

                pe.wait_ge(h_done[0], now)
                recur(0, first)
                recur(0, second)
                pe.wait_ge(h_done[1], now)
                recur(1, first).then_inc(gates_done[0], 1)
                recur(1, second).then_inc(gates_done[1], 1)
                recur(0, both_o)
                recur(1, both_o).then_inc(gates_o_done, 1)
                if t == STEPS - 1 and ahead:
                    pe.wait_ge(x_part_made, chunk + 2)
                if t < STEPS - 1 or ahead:
                    inject((t + 1) % STEPS, now)
                if ahead and 0 <= t - FIRST_PIECE_AT < len(PIECES):
                    x_product(*PIECES[t - FIRST_PIECE_AT], chunk + 1)

            pe.wait_ge(wx_made, M)
            for piece in PIECES:
                x_product(*piece, 0)
            pe.wait_ge(ident_made, 1)
            pe.wait_ge(zeroed, 2)
            pe.wait_ge(x_part_made, 1)
            inject(0)
            pe.wait_ge(wh_made, M)
            with pe.Fori(0, CHUNKS - 1) as k:
                for t in range(STEPS):
                    step(k, t, True)
            for t in range(STEPS):
                step(CHUNKS - 1, t, False)


_INS = ['x', 'cond_1024', 'L0_cond_Wx', 'L0_cond_Wh', 'L0_cond_b']


def kernel(**inputs):
    import numpy as _np
    import concourse.bacc as _bacc
    from concourse import mybir as _mybir
    from concourse.bass_utils import run_bass_kernel_spmd as _run

    nc = _bacc.Bacc("TRN2", target_bir_lowering=False, num_devices=1)
    arrays, args = {}, []
    for name in _INS:
        a = _np.ascontiguousarray(inputs[name])
        arrays[f"in_{name}_dram"] = a
        args.append(nc.dram_tensor(f"in_{name}_dram", a.shape, _mybir.dt.from_np(a.dtype), kind="ExternalInput").ap())
    shape = inputs["x"].shape
    args.append(nc.dram_tensor("out_dram", shape, _mybir.dt.float32, kind="ExternalOutput").ap())
    lstm_residual_kernel(nc, *args)
    r = _run(nc, [arrays], core_ids=[0])
    return r.results[0]["out_dram"]
```
